# Optimizing a Trainium2 kernel written in Bass

```python
import numpy as np
import jax
import jax.numpy as jnp

def _softmax(x, axis=-1):
    return jax.nn.softmax(x, axis=axis)

def _gelu(x):
    return jax.nn.gelu(x, approximate=True)

def _silu(x):
    return jax.nn.silu(x)

def _sigmoid(x):
    return jax.nn.sigmoid(x)

def _layernorm(x, axis=-1, eps=1e-05):
    m = jnp.mean(x, axis=axis, keepdims=True)
    v = jnp.var(x, axis=axis, keepdims=True)
    return (x - m) / jnp.sqrt(v + eps)

def _scatter_add(tgt, idx, src, axis=0):
    return tgt.at[idx].add(src)

def _segment_sum(src, seg, n):
    return jax.ops.segment_sum(src, seg, n)
kernel_name = 'mk_cond_seq_d2_seqx_r4_a9ae1b'

def setup_inputs(seed: int=0):
    np.random.seed(seed)
    _w = jnp.asarray

    def _rec_inputs():
        import jax
        import jax.numpy as jnp
        _rk = jax.random.key(seed)
        x = 0.5 + 0.2887 * jax.random.normal(jax.random.fold_in(_rk, 1), (4, 512, 512), jnp.float32)
        _lenS = 512 - jax.random.randint(jax.random.fold_in(_rk, 7), (4,), 0, max(1, 512 // 4) + 1, jnp.int32)
        _lenS2 = 512 - jax.random.randint(jax.random.fold_in(_rk, 8), (4,), 0, max(1, 512 // 4) + 1, jnp.int32)
        itok_B_17_1546 = jax.random.randint(jax.random.fold_in(_rk, 12), (4,), 17, 1547, jnp.int32)
        itok_B_1_2 = jax.random.randint(jax.random.fold_in(_rk, 13), (4,), 1, 3, jnp.int32)
        return (x, itok_B_17_1546, itok_B_1_2, _lenS)
    x, itok_B_17_1546, itok_B_1_2, _lenS = _rec_inputs()

    def _L0_cond_setup():
        import jax, jax.numpy as jnp
        import numpy as np
        B, T, V = (8, 128, 512)
        H = 4 * V
        key = jax.random.key(seed)
        ks = jax.random.split(key, 16)
        s = lambda n: 1.0 / np.sqrt(n)
        inp = {'x': jax.random.uniform(ks[0], (B, T, V), dtype=jnp.float32), 'lens': jax.random.randint(ks[1], (B,), 1, T, dtype=jnp.int64), 'target_codes': jax.random.randint(ks[2], (B,), 0, V, dtype=jnp.int64), 'Wq': jax.random.normal(ks[3], (V, V), jnp.float32) * s(V), 'Wk': jax.random.normal(ks[4], (V, V), jnp.float32) * s(V), 'Wv': jax.random.normal(ks[5], (V, V), jnp.float32) * s(V), 'Wp': jax.random.normal(ks[6], (V, V), jnp.float32) * s(V), 'bp': jnp.zeros((V,), jnp.float32), 'cW1': jax.random.normal(ks[7], (V, H), jnp.float32) * s(V), 'cb1': jnp.zeros((H,), jnp.float32), 'cW2': jax.random.normal(ks[8], (H, V), jnp.float32) * s(H), 'cb2': jnp.zeros((V,), jnp.float32), 'mW1': jax.random.normal(ks[9], (2 * V, H), jnp.float32) * s(2 * V), 'mb1': jnp.zeros((H,), jnp.float32), 'mW2': jax.random.normal(ks[10], (H, V), jnp.float32) * s(H), 'mb2': jnp.zeros((V,), jnp.float32)}
        return inp
    _L0_cond_all = _L0_cond_setup()
    _L0_cond_in = {k: v for k, v in _L0_cond_all.items() if k in ('Wq', 'Wk', 'Wv', 'Wp', 'bp', 'cW1', 'cb1', 'cW2', 'cb2', 'mW1', 'mb1', 'mW2', 'mb2')}
    del _L0_cond_all

    def _L1_cond_setup():
        import jax, jax.numpy as jnp
        import numpy as np
        B, S, H = (8, 512, 512)
        BN = 256
        E = 3
        LN_EPS = 1e-05
        key = jax.random.key(seed)
        ks = jax.random.split(key, 8)
        stream = jax.random.randint(ks[0], (B,), 0, E, dtype=jnp.int32)
        hidden_states = jax.random.normal(ks[1], (B, S, H), dtype=jnp.float32)
        W_down = jax.random.normal(ks[2], (E, H, BN), dtype=jnp.float32) * 0.02
        b_down = jnp.zeros((E, BN), dtype=jnp.float32)
        W_up = jax.random.normal(ks[3], (E, BN, H), dtype=jnp.float32) * 0.02
        b_up = jnp.zeros((E, H), dtype=jnp.float32)
        ln_w = jnp.ones((E, H), dtype=jnp.float32)
        ln_b = jnp.zeros((E, H), dtype=jnp.float32)
        return {'stream': stream, 'hidden_states': hidden_states, 'W_down': W_down, 'b_down': b_down, 'W_up': W_up, 'b_up': b_up, 'ln_w': ln_w, 'ln_b': ln_b}
    _L1_cond_all = _L1_cond_setup()
    _L1_cond_in = {k: v for k, v in _L1_cond_all.items() if k in ('W_down', 'b_down', 'W_up', 'b_up', 'ln_w', 'ln_b')}
    del _L1_cond_all
    return {'x': x, 'itok_B_17_1546': itok_B_17_1546, 'itok_B_1_2': itok_B_1_2, '_lenS': _lenS, 'L0_cond_Wq': _L0_cond_in['Wq'], 'L0_cond_Wk': _L0_cond_in['Wk'], 'L0_cond_Wv': _L0_cond_in['Wv'], 'L0_cond_Wp': _L0_cond_in['Wp'], 'L0_cond_bp': _L0_cond_in['bp'], 'L0_cond_cW1': _L0_cond_in['cW1'], 'L0_cond_cb1': _L0_cond_in['cb1'], 'L0_cond_cW2': _L0_cond_in['cW2'], 'L0_cond_cb2': _L0_cond_in['cb2'], 'L0_cond_mW1': _L0_cond_in['mW1'], 'L0_cond_mb1': _L0_cond_in['mb1'], 'L0_cond_mW2': _L0_cond_in['mW2'], 'L0_cond_mb2': _L0_cond_in['mb2'], 'L1_cond_W_down': _L1_cond_in['W_down'], 'L1_cond_b_down': _L1_cond_in['b_down'], 'L1_cond_W_up': _L1_cond_in['W_up'], 'L1_cond_b_up': _L1_cond_in['b_up'], 'L1_cond_ln_w': _L1_cond_in['ln_w'], 'L1_cond_ln_b': _L1_cond_in['ln_b']}

def reference(x, itok_B_17_1546, itok_B_1_2, _lenS, L0_cond_Wq, L0_cond_Wk, L0_cond_Wv, L0_cond_Wp, L0_cond_bp, L0_cond_cW1, L0_cond_cb1, L0_cond_cW2, L0_cond_cb2, L0_cond_mW1, L0_cond_mb1, L0_cond_mW2, L0_cond_mb2, L1_cond_W_down, L1_cond_b_down, L1_cond_W_up, L1_cond_b_up, L1_cond_ln_w, L1_cond_ln_b):
    import jax
    import jax.numpy as jnp

    def _L0_cond_ref(x, lens, target_codes, Wq, Wk, Wv, Wp, bp, cW1, cb1, cW2, cb2, mW1, mb1, mW2, mb2):
        import jax, jax.numpy as jnp
        import numpy as np
        B, T, V = (8, 128, 512)
        H = 4 * V
        scale = V ** (-0.5)
        q = x @ Wq
        k = x @ Wk
        v = x @ Wv
        attn = jnp.einsum('btd,bTd->btT', q, k) * scale
        attn = jax.nn.softmax(attn, axis=-1)
        attn_out = jnp.einsum('btT,bTd->btd', attn, v) @ Wp + bp
        target_embed = jax.nn.one_hot(target_codes, V, dtype=x.dtype)[:, None, :]
        cms_out = jax.nn.gelu(attn_out @ cW1 + cb1, approximate=False) @ cW2 + cb2
        cms_out = cms_out + target_embed
        concat = jnp.concatenate([attn_out, cms_out], axis=-1)
        modifier = jax.nn.gelu(concat @ mW1 + mb1, approximate=False) @ mW2 + mb2
        out = jnp.clip(x + cms_out + modifier, 0.0, 1.0)
        return out

    def _L1_cond_ref(stream, hidden_states, W_down, b_down, W_up, b_up, ln_w, ln_b):
        import jax, jax.numpy as jnp
        import numpy as np
        B, S, H = (8, 512, 512)
        BN = 256
        E = 3
        LN_EPS = 1e-05
        Wd = W_down[stream]
        bd = b_down[stream]
        Wu = W_up[stream]
        bu = b_up[stream]
        g = ln_w[stream]
        b = ln_b[stream]
        residual = hidden_states
        h = jnp.einsum('bsh,bhk->bsk', hidden_states, Wd) + bd[:, None, :]
        h = jax.nn.gelu(h, approximate=False)
        h = jnp.einsum('bsk,bkh->bsh', h, Wu) + bu[:, None, :]
        h = residual + h
        mean = jnp.mean(h, axis=-1, keepdims=True)
        var = jnp.mean(jnp.square(h - mean), axis=-1, keepdims=True)
        h = (h - mean) * jax.lax.rsqrt(var + LN_EPS)
        return h * g[:, None, :] + b[:, None, :]
    x = _L0_cond_ref(x, _lenS, itok_B_17_1546, L0_cond_Wq, L0_cond_Wk, L0_cond_Wv, L0_cond_Wp, L0_cond_bp, L0_cond_cW1, L0_cond_cb1, L0_cond_cW2, L0_cond_cb2, L0_cond_mW1, L0_cond_mb1, L0_cond_mW2, L0_cond_mb2)
    x = _L1_cond_ref(itok_B_1_2, x, L1_cond_W_down, L1_cond_b_down, L1_cond_W_up, L1_cond_b_up, L1_cond_ln_w, L1_cond_ln_b)
    return x

_drawn_inputs = setup_inputs


def setup_inputs(seed=0):
    import zlib

    import numpy as np

    out = dict(_drawn_inputs(seed))
    spreads = {'L0_cond_bp': (0.0, 0.1),
     'L0_cond_cb1': (0.0, 0.1),
     'L0_cond_cb2': (0.0, 0.1),
     'L0_cond_mb1': (0.0, 0.1),
     'L0_cond_mb2': (0.0, 0.1),
     'L1_cond_b_down': (0.0, 0.1),
     'L1_cond_b_up': (0.0, 0.1),
     'L1_cond_ln_w': (1.0, 0.2),
     'L1_cond_ln_b': (0.0, 0.1)}
    factors = {'L0_cond_Wq': 8.0, 'L0_cond_Wk': 8.0}
    for name, (base, spread) in spreads.items():
        noise = np.random.default_rng([zlib.crc32(name.encode()), seed]).standard_normal(out[name].shape)
        drawn = base * np.exp(spread * noise) if base else spread * noise
        out[name] = jnp.asarray(drawn.astype(out[name].dtype))
    for name, factor in factors.items():
        out[name] = (out[name] * factor).astype(out[name].dtype)
    return out
```

```python
import concourse.bass as bass
from concourse import mybir
from contextlib import ExitStack

P = 128


def layers_kernel(nc, x, codes, streams, Wq, Wk, Wv, Wp, bp, cW1, cb1, cW2, cb2, mW1, mb1, mW2, mb2,
                   W_down, b_down, W_up, b_up, ln_w, ln_b, out):
    F32 = mybir.dt.float32
    F32R = mybir.dt.float32r
    I32 = mybir.dt.int32
    ALU = mybir.AluOpType
    ACT = mybir.ActivationFunctionType
    AX = mybir.AxisListType

    B, T, V = x.shape
    HID = cW1.shape[1]
    BN = W_down.shape[2]
    E = W_down.shape[0]
    KT = V // P
    TT = T // P
    NBLK = HID // P
    BT = BN // P
    SCALE = float(V) ** -0.5
    LN_EPS = 1e-5
    assert KT == TT == B == 4 and V == T == 512 and BT == 2

    ctx = ExitStack()
    with ctx:
        base = -(-nc.sbuf_base // 64) * 64
        K = 1024

        def at(name, kib, shape, dt):
            return nc.alloc_sbuf_tensor_at(name, [P] + shape, dt, offset=base + kib * K)

        res = at("res", 0, [B, KT, T], F32)
        attn_hi = at("attn_hi", 32, [B, KT, T], F32R)
        attn_lo = at("attn_lo", 64, [B, KT, T], F32R)
        cms_hi = at("cms_hi", 96, [B, KT, T], F32R)
        cms_lo = at("cms_lo", 128, [B, KT, T], F32R)
        cms_acc = at("cms_acc", 128, [B, KT, T], F32)
        wsplit = at("wsplit", 160, [2, 12 * 256], F32R)
        raw = at("raw", 184, [2048], F32)
        gelu_f = at("gelu_f", 192, [2, T], F32)
        gelu_hi = at("gelu_hi", 196, [2, T], F32R)
        gelu_lo = at("gelu_lo", 200, [2, T], F32R)
        z = [at("z_even", 196, [TT, T], F32), at("z_odd", 184, [TT, T], F32)]
        Wc_hi = at("Wc_hi", 96, [KT, V], F32R)
        Wc_lo = at("Wc_lo", 104, [KT, V], F32R)
        a_hi = at("a_hi", 112, [KT, T], F32R)
        a_lo = at("a_lo", 120, [KT, T], F32R)
        Wq_raw = at("Wq_raw", 112, [KT, V], F32)
        Wk_raw = at("Wk_raw", 120, [KT, V], F32)
        M_hi = at("M_hi", 128, [KT, V], F32R)
        M_lo = at("M_lo", 136, [KT, V], F32R)
        xT_hi = at("xT_hi", 144, [KT, T], F32R)
        xT_lo = at("xT_lo", 152, [KT, T], F32R)
        xn_hi = at("xn_hi", 160, [TT, V], F32R)
        xn_lo = at("xn_lo", 168, [TT, V], F32R)
        Wv_raw = at("Wv_raw", 176, [KT, V], F32)
        Wp_raw = at("Wp_raw", 184, [KT, V], F32)
        prob = at("prob", 184, [TT, T], F32)
        x_raw = at("x_raw", 192, [TT, V], F32)

        small = [204 * K]

        def sm(name, shape, dt=F32):
            n = 4
            for d in shape:
                n *= d
            h = nc.alloc_sbuf_tensor_at(name, [P] + shape, dt, offset=base + small[0])
            small[0] += -(-n // 32) * 32
            return h

        ident = sm("ident", [P])
        ident_r = sm("ident_r", [P], F32R)
        BP, CB1, MB1, CB2, MB2, BD = 0, KT, KT + NBLK, KT + 2 * NBLK, 2 * KT + 2 * NBLK, 3 * KT + 2 * NBLK
        bias_rows = at("bias_rows", 200, [P], F32)
        bias = sm("bias", [BD + BT * B])
        cms_bias = sm("cms_bias", [B, KT])
        feature_i = sm("feature_i", [KT], I32)
        feature = sm("feature", [KT])
        codes_i = sm("codes_i", [B], I32)
        codes_f = sm("codes_f", [B])
        streams_i = sm("streams_i", [B], I32)
        streams_f = sm("streams_f", [B])
        wrap = sm("wrap", [B])
        streams_ok = sm("streams_ok", [B], I32)
        neg_max = sm("neg_max", [TT])
        row_sum = sm("row_sum", [TT])
        row_inv = sm("row_inv", [TT])
        eps = sm("eps", [1])
        gate = sm("gate", [KT])
        hidden_bias = sm("hidden_bias", [2])
        stats = sm("stats", [TT, 6])
        mean_var = sm("mean_var", [TT, 2])
        std = sm("std", [TT])
        rstd = sm("rstd", [TT])
        shift = sm("shift", [TT])

        bank = [ctx.enter_context(nc.psum_tensor(f"bank{i}", [P, 512], F32)) for i in range(8)]

        def sem(name):
            return ctx.enter_context(nc.semaphore(name))

        Wq_loaded = [sem(f"Wq_loaded{k}") for k in range(KT)]
        Wk_loaded = [sem(f"Wk_loaded{k}") for k in range(KT)]
        Wv_loaded = sem("Wv_loaded")
        Wp_loaded = sem("Wp_loaded")
        x_loaded = sem("x_loaded")
        index_loaded = sem("index_loaded")
        bias_loaded = sem("bias_loaded")
        raw_loaded = sem("raw_loaded")
        rows_loaded = sem("rows_loaded")
        stored = [[sem(f"stored_{k}_{t}") for t in range(TT)] for k in range(2)]
        const_made = sem("const_made")
        const_step = sem("const_step")
        Wp_split = sem("Wp_split")
        x_split = sem("x_split")
        w_split = sem("w_split")
        x_kept = sem("x_kept")
        res_added = sem("res_added")
        filled = sem("filled")
        bias_filled = sem("bias_filled")
        h_filled = sem("h_filled")
        out_filled = sem("out_filled")
        up_filled = sem("up_filled")
        hi_made = sem("hi_made")
        hidden_bias_made = sem("hidden_bias_made")
        w_hi_made = sem("w_hi_made")
        x_hi_made = sem("x_hi_made")
        Wp_hi_made = sem("Wp_hi_made")
        gelu_made = sem("gelu_made")
        cms_hi_made = sem("cms_hi_made")
        y_hi_made = sem("y_hi_made")
        std_made = sem("std_made")
        normed = sem("normed")
        lo_made = sem("lo_made")
        max_made = sem("max_made")
        inv_made = sem("inv_made")
        streams_made = sem("streams_made")
        stream_step = sem("stream_step")
        bias_made = sem("bias_made")
        bias_step = sem("bias_step")
        gelu_lo_made = sem("gelu_lo_made")
        summed = sem("summed")
        cms_lo_made = sem("cms_lo_made")
        clipped = sem("clipped")
        y_lo_made = sem("y_lo_made")
        z_made = sem("z_made")
        stats_made = sem("stats_made")
        var_made = sem("var_made")
        rstd_made = sem("rstd_made")
        shift_made = sem("shift_made")
        scaled = sem("scaled")
        z_done = [sem(f"z_done{t}") for t in range(TT)]

        START = 4 * KT
        XT, Q, S, PT, A, PER_BATCH = 0, 5, 10, 15, 20, 24
        FILL = (4, 9, 14, 19)

        def first(b):
            return START + PER_BATCH * b

        LAST = first(B)
        q_hi, q_lo = attn_hi[:, B - 1], attn_lo[:, B - 1]
        PT_hi, PT_lo = attn_hi[:, B - 1], attn_lo[:, B - 1]
        WqT_hi, WqT_lo = attn_hi[:, 2], attn_lo[:, 2]
        WkT_hi, WkT_lo = attn_hi[:, 3], attn_lo[:, 3]
        WvT_hi, WvT_lo = attn_hi[:, 0], attn_lo[:, 0]
        Wp_hi, Wp_lo = attn_hi[:, 1], attn_lo[:, 1]

        def cols(t):
            return slice(t * P, (t + 1) * P)

        def blocks(tile):
            return tile[:, :].rearrange("p (k c) -> p k c", k=KT)

        def f32(ap):
            return ap.bitcast(F32)

        UNITS = 2 * NBLK * B
        CMS_UNITS = NBLK * B
        PAIR = 2 * B

        def w1(slot, mod):
            o, n = (0, 8) if mod else (1024, 4)
            hi = wsplit[:, 1 - slot, o:o + n * P].rearrange("p (k c) -> p k c", k=n)
            lo = wsplit[:, 1 - slot, o + n * P:o + 2 * n * P].rearrange("p (k c) -> p k c", k=n)
            return hi, lo

        def w2(slot):
            return wsplit[:, 1 - slot, 2048:2560], wsplit[:, 1 - slot, 2560:3072]

        def down(b, part):
            return part[:, b, 0:2, :].rearrange("p a (k c) -> p (a k) c", c=BN)

        def up(b, part):
            return part[:, b, 2:4, :]

        def g1(b, lo):
            return wsplit[:, 1 - b % 2, 1024 * lo:1024 * (lo + 1)].rearrange("p (k c) -> p k c", k=BT)

        def raw_part(k):
            return raw[:, 1024 * k:1024 * (k + 1)].rearrange("p (k c) -> p k c", c=(BN, V)[k])

        raw_w1 = {False: raw[:, 0:4 * P], True: raw[:, 0:8 * P]}
        raw_w2 = raw[:, 1024:1536]

        block = ctx.enter_context(nc.Block())

        @block.sync
        def _(sp):
            def weight(w):
                return w.rearrange("(k p) n -> p k n", p=P)

            def load_x(b):
                sp.dma_start(x_raw[:, :, :], x[b].rearrange("(t p) d -> p t d", p=P)).then_inc(x_loaded, 16)

            for k in range(KT):
                sp.dma_start(Wq_raw[:, k, :], Wq[k * P:(k + 1) * P, :]).then_inc(Wq_loaded[k], 16)
            for k in range(KT):
                sp.dma_start(Wk_raw[:, k, :], Wk[k * P:(k + 1) * P, :]).then_inc(Wk_loaded[k], 16)
            sp.dma_start(Wv_raw[:, :, :], weight(Wv)).then_inc(Wv_loaded, 16)
            sp.dma_start(streams_i[:, :], streams.partition_broadcast(P)).then_inc(index_loaded, 16)
            sp.dma_start(codes_i[:, :], codes.partition_broadcast(P)).then_inc(index_loaded, 16)
            load_x(0)
            sp.dma_start(Wp_raw[:, :, :], weight(Wp)).then_inc(Wp_loaded, 16)
            sp.wait_ge(const_made, 3)
            for row, vec in ((BP, bp), (CB1, cb1), (MB1, mb1), (CB2, cb2), (MB2, mb2)):
                n = vec.shape[0] // P
                sp.dma_start(bias_rows[row:row + n, :], vec.rearrange("(k p) -> k p", p=P)).then_inc(bias_loaded, 16)
            sp.wait_ge(streams_made, 1)
            stream = [sp.value_load(streams_ok[0:1, b:b + 1], min_val=0, max_val=E - 1) for b in range(B)]
            for b in range(B):
                row = BD + BT * b
                sp.dma_start(bias_rows[row:row + BT, :],
                             b_down[bass.ds(stream[b], 1), :].rearrange("a (k p) -> (a k) p", p=P)).then_inc(bias_loaded, 16)

            for b in range(1, B):
                sp.wait_ge(filled, first(b - 1) + XT + 4)
                sp.wait_ge(x_split, TT * b)
                load_x(b)

            def load_cms(n):
                sp.dma_start(raw_w1[False].rearrange("p (k c) -> p k c", c=P),
                             cW1[:, bass.ds(n * P, P)].rearrange("(k p) c -> p k c", p=P)).then_inc(raw_loaded, 16)
                sp.dma_start(raw_w2, cW2[bass.ds(n * P, P), :]).then_inc(raw_loaded, 16)

            sp.wait_ge(filled, first(B - 1) + PT + 4)
            load_cms(0)
            with sp.Fori(1, NBLK) as n:
                sp.wait_ge(w_split, n * 2)
                load_cms(n)
            with sp.Fori(0, NBLK) as n:
                sp.wait_ge(w_split, n * 2 + 2 * NBLK)
                sp.dma_start(raw_w1[True].rearrange("p (k c) -> p k c", c=P),
                             mW1[:, bass.ds(n * P, P)].rearrange("(k p) c -> p k c", p=P)).then_inc(raw_loaded, 16)
                sp.dma_start(raw_w2, mW2[bass.ds(n * P, P), :]).then_inc(raw_loaded, 16)

            def load_adapter(b):
                sp.wait_ge(w_split, 4 * NBLK + 2 * b)
                sp.dma_start(raw[:, 0:1024].rearrange("p (k c) -> p k c", c=BN),
                             W_down[bass.ds(stream[b], 1), :, :].rearrange("a (k p) c -> p (a k) c", p=P)).then_inc(raw_loaded, 16)
                sp.dma_start(raw[:, 1024:2048].rearrange("p (k c) -> p k c", c=V),
                             W_up[bass.ds(stream[b], 1), :, :].rearrange("a (k p) c -> p (a k) c", p=P)).then_inc(raw_loaded, 16)

            def load_rows(b):
                sp.wait_ge(y_lo_made, KT * (b + 1))
                for k, vec in enumerate((b_up, ln_w, ln_b)):
                    row = vec[bass.ds(stream[b], 1), :].rearrange("a n -> (a n)")
                    sp.dma_start(res[:, b, k, :], row.partition_broadcast(P)).then_inc(rows_loaded, 16)

            def store(b):
                for t in range(TT):
                    sp.wait_ge(z_done[t], b + 1)
                    sp.dma_start(out[b, t * P:(t + 1) * P, :], z[b % 2][:, t, :]).then_inc(stored[b % 2][t], 16)

            for b in range(3):
                load_adapter(b)
            load_rows(0)
            load_rows(1)
            load_adapter(3)
            load_rows(2)
            store(0)
            load_rows(3)
            for b in range(1, B):
                store(b)
            for rows in stored:
                for t in range(TT):
                    sp.wait_ge(rows[t], 16 * B // 2)

        @block.gpsimd
        def _(pool):
            pool.memset(ident[:, :], 0.0).then_inc(const_step, 1)
            pool.memset(eps[:, :], LN_EPS).then_inc(const_made, 1)
            pool.memset(bias_rows[:, :], 0.0).then_inc(const_made, 1)
            pool.iota(feature_i[:, :], pattern=[[P, KT]], base=0, channel_multiplier=1).then_inc(const_made, 1)
            pool.wait_ge(const_step, 1)
            pool.affine_select(out=ident[:, :], in_=ident[:, :], compare_op=ALU.not_equal, fill=1.0, base=0,
                               pattern=[[-1, P]], channel_multiplier=1).then_inc(const_made, 1)
            pool.wait_ge(const_made, 4)
            pool.tensor_copy(ident_r[:, :], ident[:, :]).then_inc(const_made, 1)

            def lo(dst, src, hi, done):
                pool.tensor_tensor(dst, src, f32(hi), ALU.subtract).then_inc(done, 1)

            for k in range(KT):
                pool.wait_ge(Wp_hi_made, k + 1)
                lo(Wp_lo[:, k, :], Wp_raw[:, k, :], Wp_hi[:, k, :], Wp_split)

            def split_x(b):
                for t in range(TT):
                    pool.wait_ge(x_hi_made, b * TT + (t + 1))
                    lo(xn_lo[:, t, :], x_raw[:, t, :], xn_hi[:, t, :], x_split)
                    pool.tensor_tensor(res[:, b, :, cols(t)], f32(xT_hi[:, :, cols(t)]), f32(xT_lo[:, :, cols(t)]),
                                       ALU.add).then_inc(x_kept, 1)

            split_x(0)
            with pool.Fori(1, B) as b:
                split_x(b)

            def split_block(n, slot, mod):
                hi1, lo1 = w1(slot, mod)
                hi2, lo2 = w2(slot)
                pool.wait_ge(w_hi_made, n * 2 + 1)
                lo(lo1, raw_w1[mod].rearrange("p (k c) -> p k c", c=P), hi1, w_split)
                pool.wait_ge(w_hi_made, n * 2 + 2)
                lo(lo2, raw_w2, hi2, w_split)

            def add_cms(r):
                for m in range(KT):
                    pool.wait_ge(summed, 4 * (CMS_UNITS - B + r) + m + 1)
                    pool.tensor_tensor(res[:, r, m, :], res[:, r, m, :], cms_acc[:, r, m, :], ALU.add).then_inc(res_added, 1)

            for s in range(2):
                split_block(s, s, False)
            with pool.Fori(1, NBLK // 2) as j:
                for s in range(2):
                    split_block(j * 2 + s, s, False)
            add_cms(0)
            split_block(NBLK, 0, True)
            for r in range(1, B):
                add_cms(r)
            split_block(NBLK + 1, 1, True)
            with pool.Fori(NBLK // 2 + 1, NBLK) as j:
                for s in range(2):
                    split_block(j * 2 + s, s, True)

            for b in range(B):
                for k, part in enumerate((down, up)):
                    pool.wait_ge(w_hi_made, 4 * NBLK + 2 * b + k + 1)
                    lo(part(b, cms_lo), raw_part(k), part(b, cms_hi), w_split)
            for b in range(B):
                for t in range(TT):
                    pool.wait_ge(normed, TT * b + t + 1)
                    pool.tensor_tensor(z[b % 2][:, t, :], z[b % 2][:, t, :], res[:, b, 1, :], ALU.mult).then_inc(scaled, 1)
                    if t % 2 == 1:
                        pool.wait_ge(scaled, TT * b + t + 1)
                        pool.tensor_tensor(z[b % 2][:, t, :], z[b % 2][:, t, :], res[:, b, 2, :], ALU.add).then_inc(z_done[t], 1)

        @block.tensor
        def _(pe):
            def product(tile, terms, first_one=True, last_one=True):
                for n, ((sh, sl), (mh, ml)) in enumerate(terms):
                    pe.matmul(tile, sh, mh, start=first_one and n == 0, stop=False)
                    pe.matmul(tile, sh, ml, start=False, stop=False)
                    last = pe.matmul(tile, sl, mh, start=False, stop=last_one and n == len(terms) - 1)
                return last

            def tile_free(n):
                pe.wait_ge(lo_made, n - 7)

            def turned(n, pos, source, k):
                for c in range(KT):
                    last = pe.transpose(bank[pos % 8][:, cols(c)], source[:, k, cols(c)], ident[:, :])
                last.then_inc(filled, 1)

            def weighted(pos, hi, lo, m, moving_hi, moving_lo):
                product(bank[pos % 8][:, :], [((hi[:, k, cols(m)], lo[:, k, cols(m)]), (moving_hi[:, k, :], moving_lo[:, k, :]))
                                              for k in range(KT)]).then_inc(filled, 1)

            pe.wait_ge(const_made, 5)
            for k in range(KT):
                pe.wait_ge(Wq_loaded[k], 16)
                turned(k, k, Wq_raw, k)
            for k in range(KT):
                pe.wait_ge(Wk_loaded[k], 16)
                turned(KT + k, KT + k, Wk_raw, k)
            pe.wait_ge(lo_made, 2 * KT)
            for m in range(KT):
                weighted(2 * KT + m, WqT_hi, WqT_lo, m, WkT_hi, WkT_lo)
            pe.wait_ge(Wv_loaded, 16)
            for k in range(KT):
                tile_free(3 * KT + k)
                turned(3 * KT + k, 3 * KT + k, Wv_raw, k)

            def attn_tile(pos, m):
                weighted(pos, Wc_hi, Wc_lo, m, a_hi, a_lo)

            def batch(b, f):
                pe.wait_ge(x_loaded, b * 16 + 16)
                for k in range(TT):
                    tile_free(f + XT + k)
                    turned(f + XT + k, XT + k, x_raw, k)

                def fill(m):
                    tile_free(f + FILL[m])
                    if isinstance(b, int) and b == 0:
                        weighted(FILL[m], WvT_hi, WvT_lo, m, Wp_hi, Wp_lo)
                    else:
                        attn_tile(FILL[m], m)

                if isinstance(b, int) and b == 0:
                    pe.wait_ge(lo_made, START)
                    pe.wait_ge(Wp_split, KT)
                else:
                    pe.wait_ge(lo_made, f)
                fill(0)
                pe.wait_ge(lo_made, f + XT + 4)
                for m in range(KT):
                    tile_free(f + Q + m)
                    weighted(Q + m, M_hi, M_lo, m, xT_hi, xT_lo)
                if isinstance(b, int) and b == 0:
                    pe.wait_ge(bias_loaded, 16 * (5 + B))
                    pe.transpose(bank[3][:, 0:P], bias_rows[:, :], ident[:, :]).then_inc(bias_filled, 1)
                fill(1)
                pe.wait_ge(lo_made, f + Q + 4)
                for t in range(TT):
                    tile_free(f + S + t)
                    if isinstance(b, int) and b == 0 and (S + t) % 8 == 3:
                        pe.wait_ge(bias_made, 1)
                    weighted(S + t, q_hi, q_lo, t, xT_hi, xT_lo)
                fill(2)
                for t in range(TT):
                    pe.wait_ge(lo_made, f + (S + t + 1))
                    tile_free(f + PT + t)
                    turned(f + PT + t, PT + t, prob, t)
                fill(3)
                pe.wait_ge(lo_made, f + PT + 4)
                pe.wait_ge(x_split, b * TT + TT)
                for m in range(KT):
                    tile_free(f + A + m)
                    weighted(A + m, xn_hi, xn_lo, m, PT_hi, PT_lo)

            batch(0, first(0))
            with pe.Fori(1, B) as b:
                batch(b, b * PER_BATCH + START)
            pe.wait_ge(lo_made, LAST)
            for m in range(KT):
                tile_free(LAST + m)
                attn_tile(LAST + m, m)

            def hidden(r, s, mod):
                hi, lo = w1(s, mod)
                parts = [(attn_hi, attn_lo)] + [(cms_hi, cms_lo)] * mod
                terms = [((hi[:, KT * n + k, :], lo[:, KT * n + k, :]), (ph[:, r, k, :], pl[:, r, k, :]))
                         for n, (ph, pl) in enumerate(parts) for k in range(KT)]
                return terms

            def mlp_unit(i, n, u, mod, skip_out=False):
                r, s = u % B, u // B
                if r == 0:
                    pe.wait_ge(w_split, n * 2 + 2)
                terms = hidden(r, s, mod)
                product(bank[r][:, :], terms).then_inc(h_filled, 1)
                if not skip_out:
                    out_unit(i - 1, (u - 1) % 8)

            def out_unit(i, u):
                s, g = u // B, u % 2
                pe.wait_ge(gelu_lo_made, i + 1)
                hi, lo = w2(s)
                for m in range(KT):
                    if not (isinstance(i, int) and i == 0):
                        pe.wait_ge(summed, i * 4 + (m - 3))
                    product(bank[4 + m][:, :], [((hi[:, cols(m)], lo[:, cols(m)]), (gelu_hi[:, g, :], gelu_lo[:, g, :]))])\
                        .then_inc(out_filled, 1)

            for u in range(PAIR):
                if u < B:
                    pe.wait_ge(lo_made, LAST + u + 1)
                mlp_unit(u, u // B, u, False, skip_out=(u == 0))
            with pe.Fori(1, NBLK // 2 - 1) as j:
                for u in range(PAIR):
                    mlp_unit(j * PAIR + u, j * 2 + u // B, u, False)
            for u in range(PAIR):
                mlp_unit(CMS_UNITS - PAIR + u, NBLK - 2 + u // B, u, False)
            for u in range(PAIR):
                if u < B:
                    pe.wait_ge(cms_lo_made, KT * (u + 1))
                mlp_unit(CMS_UNITS + u, NBLK + u // B, u, True)
            with pe.Fori(NBLK // 2 + 1, NBLK - 1) as j:
                for u in range(PAIR):
                    mlp_unit(j * PAIR + u, j * 2 + u // B, u, True)
            for u in range(PAIR):
                mlp_unit(UNITS - PAIR + u, 2 * NBLK - 2 + u // B, u, True)

            def adapter_down(b):
                pe.wait_ge(y_lo_made, KT * (b + 1))
                pe.wait_ge(w_split, 4 * NBLK + 2 * (b + 1))
                dh, dl = down(b, cms_hi), down(b, cms_lo)
                for m in range(BT):
                    i = BT * b + m
                    pe.wait_ge(gelu_made, 2 * (UNITS + i - 3))
                    product(bank[i % 4][:, :], [((dh[:, k, cols(m)], dl[:, k, cols(m)]), (attn_hi[:, b, k, :], attn_lo[:, b, k, :]))
                                                for k in range(KT)]).then_inc(h_filled, 1)

            def adapter_up(b):
                uh, ul = up(b, cms_hi), up(b, cms_lo)
                gh, gl = g1(b, 0), g1(b, 1)
                pe.wait_ge(gelu_lo_made, UNITS + BT * (b + 1))
                for t in range(TT):
                    if b == 0:
                        pe.wait_ge(summed, 4 * UNITS - 3 + t)
                    else:
                        pe.wait_ge(z_made, TT * (b - 1) + t + 1)
                    tile = bank[4 + t]
                    product(tile[:, :], [((gh[:, k, cols(t)], gl[:, k, cols(t)]), (uh[:, k, :], ul[:, k, :]))
                                         for k in range(BT)], last_one=False)
                    for k in range(KT):
                        pe.matmul(tile[:, cols(k)], attn_hi[:, b, k, cols(t)], ident_r[:, :], start=False, stop=False)
                        last = pe.matmul(tile[:, cols(k)], attn_lo[:, b, k, cols(t)], ident_r[:, :], start=False, stop=(k == KT - 1))
                    last.then_inc(up_filled, 1)

            adapter_down(0)
            out_unit(UNITS - 1, PAIR - 1)
            adapter_down(1)
            adapter_up(0)
            adapter_down(2)
            adapter_up(1)
            adapter_down(3)
            adapter_up(2)
            adapter_up(3)

        @block.scalar
        def _(act):
            def copy(n, pos, dst, **kw):
                act.wait_ge(filled, n + 1)
                act.activation(dst, kw.pop("src", bank[pos % 8][:, :]), ACT.Identity if "bias" in kw else ACT.Copy, **kw).then_inc(hi_made, 1)

            def weights_hi(n, s, mod, layer):
                hi = (w1(s, mod)[0], w2(s)[0])[layer]
                act.wait_ge(raw_loaded, n * 32 + 32)
                act.activation(hi, (raw_w1[mod].rearrange("p (k c) -> p k c", c=P), raw_w2)[layer], ACT.Copy).then_inc(w_hi_made, 1)

            for k in range(KT):
                copy(k, k, WqT_hi[:, :, cols(k)], src=blocks(bank[k]))
            for k in range(KT):
                copy(KT + k, KT + k, WkT_hi[:, :, cols(k)], src=blocks(bank[4 + k]))
            for m in range(KT):
                copy(2 * KT + m, m, M_hi[:, m, :], scale=SCALE)
                act.wait_ge(Wp_loaded, 16)
                act.activation(Wp_hi[:, m, :], Wp_raw[:, m, :], ACT.Copy).then_inc(Wp_hi_made, 1)
            for k in range(KT):
                copy(3 * KT + k, 4 + k, WvT_hi[:, :, cols(k)], src=blocks(bank[4 + k]))

            def batch(b, f):
                zero = isinstance(b, int) and b == 0

                def fill(m):
                    pos = FILL[m]
                    if zero:
                        copy(f + pos, pos, Wc_hi[:, m, :])
                    else:
                        act.wait_ge(filled, f + (pos + 1))
                        act.activation(gate[:, m:m + 1], eps[:, :], ACT.Copy)
                        act.activation(attn_hi[:, b - 1, m, :], bank[pos % 8][:, :], ACT.Identity,
                                       bias=bias[:, BP + m:BP + m + 1]).then_inc(hi_made, 1)

                for k in range(TT):
                    tile = blocks(bank[(XT + k) % 8])
                    act.wait_ge(filled, f + (XT + k + 1))
                    if not zero and k == 0:
                        act.wait_ge(x_kept, b * TT)
                    act.activation(xT_hi[:, :, cols(k)], tile, ACT.Copy).then_inc(hi_made, 1)
                fill(0)
                for m in range(KT):
                    copy(f + Q + m, Q + m, q_hi[:, m, :])
                fill(1)
                for t in range(TT):
                    act.wait_ge(max_made, b * TT + (t + 1))
                    act.activation(prob[:, t, :], bank[(S + t) % 8][:, :], ACT.Exp, bias=neg_max[:, t:t + 1],
                                   accum_out=row_sum[:, t:t + 1]).then_inc(hi_made, 1)
                    act.activation(xn_hi[:, t, :], x_raw[:, t, :], ACT.Copy).then_inc(x_hi_made, 1)
                fill(2)
                for t in range(TT):
                    copy(f + PT + t, PT + t, PT_hi[:, :, cols(t)], src=blocks(bank[(PT + t) % 8]))
                fill(3)
                for m in range(KT):
                    copy(f + A + m, A + m, a_hi[:, m, :])

            batch(0, first(0))
            with act.Fori(1, B) as b:
                batch(b, b * PER_BATCH + START)
            for layer in range(2):
                weights_hi(0, 0, False, layer)
            for m in range(KT):
                copy(LAST + m, LAST + m, attn_hi[:, B - 1, m, :], bias=bias[:, BP + m:BP + m + 1])

            def fetch_bias(n, s):
                act.activation(hidden_bias[:, s:s + 1], bias[:, bass.ds(n + CB1, 1)], ACT.Copy).then_inc(hidden_bias_made, 1)

            def gelu_unit(i, n, u, mod):
                g, r, s = u % 2, u % B, u // B
                if r == 0:
                    act.wait_ge(hidden_bias_made, n + 1)
                act.wait_ge(h_filled, i + 1)
                if not (isinstance(i, int) and i < 2):
                    act.wait_ge(gelu_lo_made, i - 1)
                    act.wait_ge(out_filled, i * 4 - 4)
                for dst in (gelu_f, gelu_hi):
                    act.activation(dst[:, g, :], bank[r][:, :], ACT.Gelu, bias=hidden_bias[:, s:s + 1]).then_inc(gelu_made, 1)
                if isinstance(n, int) and n == 2 * NBLK - 1:
                    return
                if r == 1 or r == 2:
                    weights_hi(n + 1, 1 - s, mod or (isinstance(n, int) and n == NBLK - 1), r - 1)
                if r == 3:
                    fetch_bias(n + 1, 1 - s)

            def pair(i0, n0, mod):
                for u in range(PAIR):
                    gelu_unit(i0 + u, n0 + u // B, u, mod)

            def cms_final(r):
                for m in range(KT):
                    act.wait_ge(summed, 4 * (CMS_UNITS - B + r) + m + 1)
                    act.activation(cms_hi[:, r, m, :], cms_acc[:, r, m, :], ACT.Copy).then_inc(cms_hi_made, 1)

            def adapter_hi(b):
                act.wait_ge(raw_loaded, 32 * (2 * NBLK + b + 1))
                for k, part in enumerate((down, up)):
                    act.activation(part(b, cms_hi), raw_part(k), ACT.Copy).then_inc(w_hi_made, 1)

            def y_final(r):
                for m in range(KT):
                    act.wait_ge(clipped, KT * r + m + 1)
                    act.activation(attn_hi[:, r, m, :], res[:, r, m, :], ACT.Copy).then_inc(y_hi_made, 1)

            fetch_bias(0, 0)
            pair(0, 0, False)
            with act.Fori(1, NBLK // 2 - 1) as j:
                pair(j * PAIR, j * 2, False)
            for u in range(PAIR):
                gelu_unit(CMS_UNITS - PAIR + u, NBLK - 2 + u // B, u, False)
                if u > B:
                    cms_final(u - B - 1)
            for u in range(PAIR):
                gelu_unit(CMS_UNITS + u, NBLK + u // B, u, True)
                if u == 0:
                    cms_final(B - 1)
            with act.Fori(NBLK // 2 + 1, NBLK - 1) as j:
                pair(j * PAIR, j * 2, True)
            for u in range(PAIR):
                gelu_unit(UNITS - PAIR + u, 2 * NBLK - 2 + u // B, u, True)
                if u > B:
                    y_final(u - B - 1)
                if u >= B and u != B + 2:
                    adapter_hi(min(u - B, 2))

            def gelu_adapter(b):
                for m in range(BT):
                    i = UNITS + BT * b + m
                    c = BD + BT * b + m
                    act.wait_ge(h_filled, i + 1)
                    act.wait_ge(gelu_lo_made, i - 1)
                    if b < 2:
                        act.wait_ge(out_filled, 4 * (UNITS - B * (1 - b)))
                    else:
                        act.wait_ge(up_filled, TT * (b - 1))
                    act.activation(gelu_f[:, m, :], bank[i % 4][:, :], ACT.Gelu, bias=bias[:, c:c + 1]).then_inc(gelu_made, 1)
                    act.activation(g1(b, 0)[:, m, :], bank[i % 4][:, :], ACT.Gelu, bias=bias[:, c:c + 1]).then_inc(gelu_made, 1)

            def norm(b):
                for t in range(TT):
                    n = TT * b + t
                    act.wait_ge(var_made, n + 1)
                    act.activation(std[:, t:t + 1], mean_var[:, t, 1:2], ACT.Sqrt, bias=eps[:, :]).then_inc(std_made, 1)
                    act.wait_ge(shift_made, n + 1)
                    act.activation(z[b % 2][:, t, :], z[b % 2][:, t, :], ACT.Identity, bias=shift[:, t:t + 1], scale=rstd[:, t:t + 1]).then_inc(normed, 1)

            gelu_adapter(0)
            y_final(B - 1)
            adapter_hi(3)
            gelu_adapter(1)
            norm(0)
            gelu_adapter(2)
            norm(1)
            gelu_adapter(3)
            norm(2)
            norm(3)

        @block.vector
        def _(dve):
            def lo(n, dst, src, hi):
                dve.wait_ge(hi_made, n + 1)
                dve.tensor_tensor(dst, src, f32(hi), ALU.subtract).then_inc(lo_made, 1)

            def lo_biased(n, dst, src, column, hi):
                dve.wait_ge(hi_made, n + 1)
                dve.scalar_tensor_tensor(dst, src, column, f32(hi), ALU.add, ALU.subtract).then_inc(lo_made, 1)

            for k in range(KT):
                lo(k, WqT_lo[:, :, cols(k)], blocks(bank[k]), WqT_hi[:, :, cols(k)])
            for k in range(KT):
                lo(KT + k, WkT_lo[:, :, cols(k)], blocks(bank[4 + k]), WkT_hi[:, :, cols(k)])
            dve.wait_ge(index_loaded, 32)
            dve.tensor_copy(streams_f[:, :], streams_i[:, :]).then_inc(stream_step, 1)
            dve.wait_ge(stream_step, 1)
            dve.tensor_scalar(wrap[:, :], streams_f[:, :], 0.0, float(E), ALU.is_lt, ALU.mult).then_inc(stream_step, 1)
            dve.wait_ge(stream_step, 2)
            dve.tensor_tensor(wrap[:, :], wrap[:, :], streams_f[:, :], ALU.add).then_inc(stream_step, 1)
            dve.wait_ge(stream_step, 3)
            dve.tensor_scalar(streams_ok[:, :], wrap[:, :], 0.0, float(E - 1), ALU.max, ALU.min).then_inc(streams_made, 1)

            for m in range(KT):
                n = 2 * KT + m
                dve.wait_ge(hi_made, n + 1)
                dve.scalar_tensor_tensor(M_lo[:, m, :], bank[m][:, :], SCALE, f32(M_hi[:, m, :]), ALU.mult, ALU.subtract)\
                   .then_inc(lo_made, 1)
            for k in range(KT):
                lo(3 * KT + k, WvT_lo[:, :, cols(k)], blocks(bank[4 + k]), WvT_hi[:, :, cols(k)])

            def make_biases():
                dve.wait_ge(bias_filled, 1)
                dve.tensor_copy(bias[:, :], bank[3][:, 0:BD + BT * B]).then_inc(bias_made, 1)
                dve.wait_ge(const_made, 5)
                dve.tensor_copy(feature[:, :], feature_i[:, :]).then_inc(bias_step, 1)
                dve.tensor_copy(codes_f[:, :], codes_i[:, :]).then_inc(bias_step, 1)
                dve.wait_ge(bias_step, 2)
                dve.wait_ge(bias_made, 1)
                for b in range(B):
                    dve.scalar_tensor_tensor(cms_bias[:, b, :], feature[:, :], codes_f[:, b:b + 1], bias[:, CB2:CB2 + KT],
                                             ALU.is_equal, ALU.add).then_inc(bias_step, 1)

            def batch(b, f):
                zero = isinstance(b, int) and b == 0

                def fill(m):
                    pos = FILL[m]
                    if zero:
                        lo(f + pos, Wc_lo[:, m, :], bank[pos % 8][:, :], Wc_hi[:, m, :])
                    else:
                        lo_biased(f + pos, attn_lo[:, b - 1, m, :], bank[pos % 8][:, :], bias[:, BP + m:BP + m + 1],
                                  attn_hi[:, b - 1, m, :])

                for k in range(TT):
                    lo(f + (XT + k), xT_lo[:, :, cols(k)], blocks(bank[(XT + k) % 8]), xT_hi[:, :, cols(k)])
                fill(0)
                for m in range(KT):
                    lo(f + (Q + m), q_lo[:, m, :], bank[(Q + m) % 8][:, :], q_hi[:, m, :])
                if zero:
                    make_biases()
                fill(1)
                for t in range(TT):
                    dve.wait_ge(filled, f + (S + t + 1))
                    dve.reduce_max(neg_max[:, t:t + 1], bank[(S + t) % 8][:, :], AX.X, negate=True).then_inc(max_made, 1)
                    dve.wait_ge(hi_made, f + (S + t + 1))
                    dve.reciprocal(row_inv[:, t:t + 1], row_sum[:, t:t + 1]).then_inc(inv_made, 1)
                    dve.wait_ge(inv_made, b * TT + (t + 1))
                    dve.tensor_scalar(prob[:, t, :], prob[:, t, :], row_inv[:, t:t + 1], None, ALU.mult).then_inc(lo_made, 1)
                fill(2)
                for t in range(TT):
                    lo(f + (PT + t), PT_lo[:, :, cols(t)], blocks(bank[(PT + t) % 8]), PT_hi[:, :, cols(t)])
                fill(3)
                for m in range(KT):
                    lo(f + (A + m), a_lo[:, m, :], bank[(A + m) % 8][:, :], a_hi[:, m, :])

            batch(0, first(0))
            with dve.Fori(1, B) as b:
                batch(b, b * PER_BATCH + START)
            for m in range(KT):
                lo_biased(LAST + m, attn_lo[:, B - 1, m, :], bank[m][:, :], bias[:, BP + m:BP + m + 1], attn_hi[:, B - 1, m, :])

            def gelu_lo_unit(i, g):
                dve.wait_ge(gelu_made, i * 2 + 2)
                dve.tensor_tensor(gelu_lo[:, g, :], gelu_f[:, g, :], f32(gelu_hi[:, g, :]), ALU.subtract).then_inc(gelu_lo_made, 1)

            def add_unit(i, r, total, start=None):
                for m in range(KT):
                    dst, src = total[:, r, m, :], bank[4 + m][:, :]
                    dve.wait_ge(out_filled, i * 4 + (m + 1))
                    if start == "cms":
                        op = dve.tensor_scalar(dst, src, cms_bias[:, r, m:m + 1], None, ALU.add)
                    elif start == "mod":
                        if m == 0:
                            dve.wait_ge(res_added, KT * (r + 1))
                        op = dve.scalar_tensor_tensor(dst, src, bias[:, MB2 + m:MB2 + m + 1], dst, ALU.add, ALU.add)
                    else:
                        op = dve.tensor_tensor(dst, src, dst, ALU.add)
                    op.then_inc(summed, 1)

            def cms_final(r):
                for m in range(KT):
                    dve.wait_ge(cms_hi_made, KT * r + m + 1)
                    dve.wait_ge(res_added, KT * r + m + 1)
                    dve.tensor_tensor(cms_lo[:, r, m, :], cms_acc[:, r, m, :], f32(cms_hi[:, r, m, :]), ALU.subtract)\
                       .then_inc(cms_lo_made, 1)

            def clip(r):
                for m in range(KT):
                    dve.wait_ge(summed, 4 * (UNITS - B + r) + m + 1)
                    dve.tensor_scalar(res[:, r, m, :], res[:, r, m, :], 0.0, 1.0, ALU.max, ALU.min).then_inc(clipped, 1)

            def y_final(r):
                for m in range(KT):
                    dve.wait_ge(y_hi_made, KT * r + m + 1)
                    dve.tensor_tensor(attn_lo[:, r, m, :], res[:, r, m, :], f32(attn_hi[:, r, m, :]), ALU.subtract)\
                       .then_inc(y_lo_made, 1)

            dve.wait_ge(bias_step, 2 + B)
            for i in range(PAIR):
                if i > 0:
                    add_unit(i - 1, (i - 1) % B, cms_acc, start="cms" if i - 1 < B else None)
                gelu_lo_unit(i, i % 2)
            with dve.Fori(1, NBLK // 2 - 1) as j:
                for u in range(PAIR):
                    add_unit(j * PAIR + (u - 1), (u - 1) % B, cms_acc)
                    gelu_lo_unit(j * PAIR + u, u % 2)
            for u in range(PAIR):
                i = CMS_UNITS - PAIR + u
                add_unit(i - 1, (u - 1) % B, cms_acc)
                gelu_lo_unit(i, u % 2)
                if u > B + 1:
                    cms_final(u - B - 2)
            for u in range(PAIR):
                i = CMS_UNITS + u
                if u == 0:
                    add_unit(i - 1, B - 1, cms_acc)
                else:
                    add_unit(i - 1, (u - 1) % B, res, start="mod" if u - 1 < B else None)
                gelu_lo_unit(i, u % 2)
                if u < 2:
                    cms_final(B - 2 + u)
            with dve.Fori(NBLK // 2 + 1, NBLK - 1) as j:
                for u in range(PAIR):
                    add_unit(j * PAIR + (u - 1), (u - 1) % B, res)
                    gelu_lo_unit(j * PAIR + u, u % 2)
            for u in range(PAIR):
                i = UNITS - PAIR + u
                add_unit(i - 1, (u - 1) % B, res)
                if u > B:
                    clip(u - B - 1)
                gelu_lo_unit(i, u % 2)
                if u > B + 1:
                    y_final(u - B - 2)

            def gelu_lo_adapter(b):
                for m in range(BT):
                    dve.wait_ge(gelu_made, 2 * (UNITS + BT * b + m + 1))
                    dve.tensor_tensor(g1(b, 1)[:, m, :], gelu_f[:, m, :], f32(g1(b, 0)[:, m, :]), ALU.subtract)\
                       .then_inc(gelu_lo_made, 1)

            def finish_row(n):
                b, t = n // TT, n % TT
                dve.wait_ge(scaled, n + 1)
                dve.tensor_tensor(z[b % 2][:, t, :], z[b % 2][:, t, :], res[:, b, 2, :], ALU.add).then_inc(z_done[t], 1)

            def layer_norm(b):
                dve.wait_ge(rows_loaded, 48 * (b + 1))
                for t in range(TT):
                    n = TT * b + t
                    dve.wait_ge(up_filled, n + 1)
                    if b == 1 and t == 0:
                        dve.wait_ge(w_split, 4 * NBLK + 2 * B)
                    if b > 1:
                        dve.wait_ge(stored[b % 2][t], 16 * (b // 2))
                    dve.tensor_tensor(z[b % 2][:, t, :], bank[4 + t][:, :], res[:, b, 0, :], ALU.add).then_inc(z_made, 1)
                    dve.wait_ge(z_made, n + 1)
                    dve.bn_stats(stats[:, t, :], z[b % 2][:, t, :]).then_inc(stats_made, 1)
                    dve.wait_ge(stats_made, n + 1)
                    dve.bn_aggr(mean_var[:, t, :], stats[:, t, :]).then_inc(var_made, 1)
                    if n > 1 and n % 2 == 0:
                        finish_row(n - 2)
                    dve.wait_ge(std_made, n + 1)
                    dve.reciprocal(rstd[:, t:t + 1], std[:, t:t + 1]).then_inc(rstd_made, 1)
                    dve.wait_ge(rstd_made, n + 1)
                    dve.tensor_scalar(shift[:, t:t + 1], mean_var[:, t, 0:1], rstd[:, t:t + 1], -1.0, ALU.mult, ALU.mult)\
                       .then_inc(shift_made, 1)

            add_unit(UNITS - 1, B - 1, res)
            clip(B - 1)
            y_final(B - 2)
            gelu_lo_adapter(0)
            y_final(B - 1)
            for b in range(B):
                if b < B - 1:
                    gelu_lo_adapter(b + 1)
                layer_norm(b)
            finish_row(B * TT - 2)


_INS = {"x": "x", "itok_B_17_1546": "codes", "itok_B_1_2": "streams",
        "L0_cond_Wq": "Wq", "L0_cond_Wk": "Wk", "L0_cond_Wv": "Wv", "L0_cond_Wp": "Wp", "L0_cond_bp": "bp",
        "L0_cond_cW1": "cW1", "L0_cond_cb1": "cb1", "L0_cond_cW2": "cW2", "L0_cond_cb2": "cb2",
        "L0_cond_mW1": "mW1", "L0_cond_mb1": "mb1", "L0_cond_mW2": "mW2", "L0_cond_mb2": "mb2",
        "L1_cond_W_down": "W_down", "L1_cond_b_down": "b_down", "L1_cond_W_up": "W_up", "L1_cond_b_up": "b_up",
        "L1_cond_ln_w": "ln_w", "L1_cond_ln_b": "ln_b"}


def kernel(**inputs):
    import numpy as _np
    import concourse.bacc as _bacc
    from concourse import mybir as _mybir
    from concourse.bass_utils import run_bass_kernel_spmd as _run

    nc = _bacc.Bacc("TRN2", target_bir_lowering=False, num_devices=1)
    arrays, args = {}, {}
    for name, short in _INS.items():
        a = _np.ascontiguousarray(inputs[name])
        arrays[f"{short}_dram"] = a
        args[short] = nc.dram_tensor(f"{short}_dram", a.shape, _mybir.dt.from_np(a.dtype), kind="ExternalInput").ap()
    shape = inputs["x"].shape
    args["out"] = nc.dram_tensor("out_dram", shape, _mybir.dt.float32, kind="ExternalOutput").ap()
    layers_kernel(nc, **args)
    r = _run(nc, [arrays], core_ids=[0])
    return r.results[0]["out_dram"]
```
